# Optimizing a Trainium2 kernel written in Bass

```python
import numpy as np
import jax
import jax.numpy as jnp

def _softmax(x, axis=-1):
    return jax.nn.softmax(x, axis=axis)

def _gelu(x):
    return jax.nn.gelu(x, approximate=True)

def _silu(x):
    return jax.nn.silu(x)

def _sigmoid(x):
    return jax.nn.sigmoid(x)

def _layernorm(x, axis=-1, eps=1e-05):
    m = jnp.mean(x, axis=axis, keepdims=True)
    v = jnp.var(x, axis=axis, keepdims=True)
    return (x - m) / jnp.sqrt(v + eps)

def _scatter_add(tgt, idx, src, axis=0):
    return tgt.at[idx].add(src)

def _segment_sum(src, seg, n):
    return jax.ops.segment_sum(src, seg, n)
kernel_name = 'mk_lm_tower_d1_tok_ids768_r4_711b19'

def setup_inputs(seed: int=0):
    np.random.seed(seed)
    _w = jnp.asarray

    def _rec_inputs():
        import jax
        import jax.numpy as jnp
        _rk = jax.random.key(seed)
        x = jax.random.randint(jax.random.fold_in(_rk, 1), (4, 2048), 0, 128, jnp.int32)
        return x
    x = _rec_inputs()

    def _L0_tok_setup():
        import jax, jax.numpy as jnp
        import numpy as np
        V, H, P = (50257, 192, 2048)
        B, S = (8, 2048)
        NEXT_TOKEN_ID = 2
        EPS = 1e-12

        def _position_indices(input_ids):
            starts = jnp.roll(input_ids == NEXT_TOKEN_ID, 1, axis=-1)
            starts = starts.at[:, 0].set(False)
            instructions = jnp.cumsum(starts.astype(jnp.int32), axis=-1)
            pos = jnp.arange(S, dtype=jnp.int32)[None, :]
            last_start = jax.lax.cummax(jnp.where(starts, pos, 0), axis=1)
            arguments = pos - last_start
            return (instructions, arguments)
        key = jax.random.key(seed)
        k0, k1, k2, k3 = jax.random.split(key, 4)
        input_ids = jax.random.randint(k0, (B, S), 0, 128, dtype=jnp.int32)
        token_emb = jax.random.normal(k1, (V, H), dtype=jnp.float32) * 0.02
        instr_emb = jax.random.normal(k2, (P, H), dtype=jnp.float32) * 0.02
        arg_emb = jax.random.normal(k3, (P, H), dtype=jnp.float32) * 0.02
        norm_w = jnp.ones((H,), dtype=jnp.float32)
        norm_b = jnp.zeros((H,), dtype=jnp.float32)
        return {'input_ids': input_ids, 'token_emb': token_emb, 'instr_emb': instr_emb, 'arg_emb': arg_emb, 'norm_w': norm_w, 'norm_b': norm_b}
    _L0_tok_all = _L0_tok_setup()
    _L0_tok_in = {k: v for k, v in _L0_tok_all.items() if k in ('token_emb', 'instr_emb', 'arg_emb', 'norm_w', 'norm_b')}
    del _L0_tok_all

    def _L0_attn_setup():
        import jax, jax.numpy as jnp
        import numpy as np
        EMBED_DIM = 192
        NUM_HEADS = 12
        HEAD_DIM = EMBED_DIM // NUM_HEADS
        SCALING = HEAD_DIM ** (-0.5)
        B, S = (2, 512)
        key = jax.random.key(seed)
        k1, k2, k3 = jax.random.split(key, 3)
        x_q = jax.random.normal(k1, (B, S, EMBED_DIM), dtype=jnp.float32)
        lim_qkv = (6.0 / (EMBED_DIM + 3 * EMBED_DIM)) ** 0.5
        lim_out = (6.0 / (2 * EMBED_DIM)) ** 0.5
        w_qkv = jax.random.uniform(k2, (3 * EMBED_DIM, EMBED_DIM), jnp.float32, -lim_qkv, lim_qkv)
        b_qkv = jnp.zeros((3 * EMBED_DIM,), jnp.float32)
        w_out = jax.random.uniform(k3, (EMBED_DIM, EMBED_DIM), jnp.float32, -lim_out, lim_out)
        b_out = jnp.zeros((EMBED_DIM,), jnp.float32)
        return {'x_q': x_q, 'w_qkv': w_qkv, 'b_qkv': b_qkv, 'w_out': w_out, 'b_out': b_out}
    _L0_attn_all = _L0_attn_setup()
    _L0_attn_in = {k: v for k, v in _L0_attn_all.items() if k in ('w_qkv', 'b_qkv', 'w_out', 'b_out')}
    del _L0_attn_all

    def _L0_ffn_setup():
        import math
        import jax, jax.numpy as jnp
        import numpy as np
        B, L, D = (8, 1024, 192)
        E = 16
        TOP_K = 2
        F_EXP = 4 * D
        F_SH = F_EXP * 2 // 4
        key = jax.random.key(seed)
        ks = jax.random.split(key, 8)
        s = lambda fan_in: 1.0 / math.sqrt(fan_in)
        return {'hidden_states': jax.random.normal(ks[0], (B, L, D), jnp.float32), 'gate_weight': jax.random.uniform(ks[1], (E, D), jnp.float32, -s(D), s(D)), 'Wg': jax.random.uniform(ks[2], (E, F_EXP, D), jnp.float32, -s(D), s(D)), 'Wu': jax.random.uniform(ks[3], (E, F_EXP, D), jnp.float32, -s(D), s(D)), 'Wd': jax.random.uniform(ks[4], (E, D, F_EXP), jnp.float32, -s(F_EXP), s(F_EXP)), 'Ws_g': jax.random.uniform(ks[5], (F_SH, D), jnp.float32, -s(D), s(D)), 'Ws_u': jax.random.uniform(ks[6], (F_SH, D), jnp.float32, -s(D), s(D)), 'Ws_d': jax.random.uniform(ks[7], (D, F_SH), jnp.float32, -s(F_SH), s(F_SH))}
    _L0_ffn_all = _L0_ffn_setup()
    _L0_ffn_in = {k: v for k, v in _L0_ffn_all.items() if k in ('gate_weight', 'Wg', 'Wu', 'Wd', 'Ws_g', 'Ws_u', 'Ws_d')}
    del _L0_ffn_all
    return {'x': x, 'L0_tok_token_emb': _L0_tok_in['token_emb'], 'L0_tok_instr_emb': _L0_tok_in['instr_emb'], 'L0_tok_arg_emb': _L0_tok_in['arg_emb'], 'L0_tok_norm_w': _L0_tok_in['norm_w'], 'L0_tok_norm_b': _L0_tok_in['norm_b'], 'L0_attn_w_qkv': _L0_attn_in['w_qkv'], 'L0_attn_b_qkv': _L0_attn_in['b_qkv'], 'L0_attn_w_out': _L0_attn_in['w_out'], 'L0_attn_b_out': _L0_attn_in['b_out'], 'L0_ffn_gate_weight': _L0_ffn_in['gate_weight'], 'L0_ffn_Wg': _L0_ffn_in['Wg'], 'L0_ffn_Wu': _L0_ffn_in['Wu'], 'L0_ffn_Wd': _L0_ffn_in['Wd'], 'L0_ffn_Ws_g': _L0_ffn_in['Ws_g'], 'L0_ffn_Ws_u': _L0_ffn_in['Ws_u'], 'L0_ffn_Ws_d': _L0_ffn_in['Ws_d']}

def reference(x, L0_tok_token_emb, L0_tok_instr_emb, L0_tok_arg_emb, L0_tok_norm_w, L0_tok_norm_b, L0_attn_w_qkv, L0_attn_b_qkv, L0_attn_w_out, L0_attn_b_out, L0_ffn_gate_weight, L0_ffn_Wg, L0_ffn_Wu, L0_ffn_Wd, L0_ffn_Ws_g, L0_ffn_Ws_u, L0_ffn_Ws_d):
    import jax
    import jax.numpy as jnp

    def _L0_tok_ref(input_ids, token_emb, instr_emb, arg_emb, norm_w, norm_b):
        import jax, jax.numpy as jnp
        import numpy as np
        V, H, P = (50257, 192, 2048)
        B, S = (8, 2048)
        NEXT_TOKEN_ID = 2
        EPS = 1e-12

        def _position_indices(input_ids):
            starts = jnp.roll(input_ids == NEXT_TOKEN_ID, 1, axis=-1)
            starts = starts.at[:, 0].set(False)
            instructions = jnp.cumsum(starts.astype(jnp.int32), axis=-1)
            pos = jnp.arange(S, dtype=jnp.int32)[None, :]
            last_start = jax.lax.cummax(jnp.where(starts, pos, 0), axis=1)
            arguments = pos - last_start
            return (instructions, arguments)
        instructions, arguments = _position_indices(input_ids)
        emb = token_emb[input_ids] + instr_emb[instructions] + arg_emb[arguments]
        mu = jnp.mean(emb, axis=-1, keepdims=True)
        var = jnp.mean(jnp.square(emb - mu), axis=-1, keepdims=True)
        out = (emb - mu) * jax.lax.rsqrt(var + EPS) * norm_w + norm_b
        return out

    def _L0_attn_ref(x_q, w_qkv, b_qkv, w_out, b_out):
        import jax, jax.numpy as jnp
        import numpy as np
        EMBED_DIM = 192
        NUM_HEADS = 12
        HEAD_DIM = EMBED_DIM // NUM_HEADS
        SCALING = HEAD_DIM ** (-0.5)
        B, S = (2, 512)
        b_sz, s_len, _ = x_q.shape
        qkv = x_q @ w_qkv.T + b_qkv
        qkv = qkv.reshape(b_sz, s_len, 3, NUM_HEADS, HEAD_DIM)
        q = qkv[:, :, 0].transpose(0, 2, 1, 3) * SCALING
        k = qkv[:, :, 1].transpose(0, 2, 1, 3)
        v = qkv[:, :, 2].transpose(0, 2, 1, 3)
        attn = jnp.einsum('bhsd,bhtd->bhst', q, k)
        attn = jax.nn.softmax(attn.astype(jnp.float32), axis=-1).astype(attn.dtype)
        out = jnp.einsum('bhst,bhtd->bhsd', attn, v)
        out = out.transpose(0, 2, 1, 3).reshape(b_sz, s_len, EMBED_DIM)
        return out @ w_out.T + b_out

    def _L0_ffn_ref(hidden_states, gate_weight, Wg, Wu, Wd, Ws_g, Ws_u, Ws_d):
        import math
        import jax, jax.numpy as jnp
        import numpy as np
        B, L, D = (8, 1024, 192)
        E = 16
        TOP_K = 2
        F_EXP = 4 * D
        F_SH = F_EXP * 2 // 4
        b, l, d = hidden_states.shape
        n = b * l
        x = hidden_states.reshape(n, d)
        scores = jax.nn.sigmoid(x @ gate_weight.T)
        capacity = math.ceil(n / E * TOP_K)
        topk_score, topk_ids = jax.lax.top_k(scores.T, capacity)
        xg = x[topk_ids]
        gate = jax.nn.silu(jnp.einsum('ecd,efd->ecf', xg, Wg))
        up = jnp.einsum('ecd,efd->ecf', xg, Wu)
        out = jnp.einsum('ecf,edf->ecd', gate * up, Wd)
        out = out * topk_score[..., None]
        y = jnp.zeros((n, d), x.dtype).at[topk_ids.reshape(-1)].add(out.reshape(-1, d))
        y = y.reshape(b, l, d)
        shared = jax.nn.silu(hidden_states @ Ws_g.T) * (hidden_states @ Ws_u.T) @ Ws_d.T
        return y + shared
    h = _L0_tok_ref(x, L0_tok_token_emb, L0_tok_instr_emb, L0_tok_arg_emb, L0_tok_norm_w, L0_tok_norm_b)
    h = h + _L0_attn_ref(_layernorm(h, axis=-1), L0_attn_w_qkv, L0_attn_b_qkv, L0_attn_w_out, L0_attn_b_out)
    h = h + _L0_ffn_ref(_layernorm(h, axis=-1), L0_ffn_gate_weight, L0_ffn_Wg, L0_ffn_Wu, L0_ffn_Wd, L0_ffn_Ws_g, L0_ffn_Ws_u, L0_ffn_Ws_d)
    return h

_drawn_inputs = setup_inputs


def setup_inputs(seed=0):
    import zlib

    import numpy as np

    out = dict(_drawn_inputs(seed))
    spreads = {'L0_tok_norm_w': (1.0, 0.2),
     'L0_tok_norm_b': (0.0, 0.1),
     'L0_attn_b_qkv': (0.0, 0.1),
     'L0_attn_b_out': (0.0, 0.1)}
    factors = {}
    for name, (base, spread) in spreads.items():
        noise = np.random.default_rng([zlib.crc32(name.encode()), seed]).standard_normal(out[name].shape)
        drawn = base * np.exp(spread * noise) if base else spread * noise
        out[name] = jnp.asarray(drawn.astype(out[name].dtype))
    for name, factor in factors.items():
        out[name] = (out[name] * factor).astype(out[name].dtype)
    return out
```

```python
from contextlib import ExitStack

import concourse.bass as bass
from concourse import mybir

F32 = mybir.dt.float32
BF16 = mybir.dt.bfloat16
I32 = mybir.dt.int32
ALU = mybir.AluOpType
ACT = mybir.ActivationFunctionType
AX = mybir.AxisListType

P = 128
TC = 4
CH = TC * P
D = 192
D2 = D - P
HD = 16
HEADS = D // HD
VW = 32
NEXT_TOKEN = 2
EPS_TOK = 1e-12
EPS_LN = 1e-5
AHEAD = 3
TERMS_Q = (0, 0, 0, 1, 1, 2)
TERMS_K = (0, 1, 2, 0, 1, 0)
SK = len(TERMS_Q) * HD
SM = SK + 2


class Chain:

    def __init__(self, engine, sem, base=0):
        self.engine, self.sem, self.base, self.n = engine, sem, base, 0

    def link(self, instruction, passed=None):
        self.n += 1
        instruction.then_inc(self.sem, 1)
        self.engine.wait_ge(self.sem, self.base + self.n)
        if passed is not None:
            hold(self.engine, passed)


def hold(engine, passed):
    engine.sem_inc(passed, 1)


def make_identity(nc, pool, ident, made):
    nc.gpsimd.memset(ident[:, :], 0.0).then_inc(made, 1)
    pool.wait_ge(made, 1)
    nc.gpsimd.affine_select(out=ident[:, :], in_=ident[:, :], compare_op=ALU.not_equal, fill=1.0, base=0,
                            pattern=[[-1, P]], channel_multiplier=1).then_inc(made, 1)


def inverse_std(nc, dve, chain, mv, eps, rs, tmp, var_ready, root_ready, n, meanwhile=None):
    ve = tmp[:, 0, :]
    t = tmp[:, 1, :]
    nc.vector.tensor_scalar(out=ve, in0=mv[:, :, 1], scalar1=eps, scalar2=None, op0=ALU.add).then_inc(var_ready, 1)
    if meanwhile:
        meanwhile()
    dve.wait_ge(root_ready, n)
    chain.link(nc.vector.reciprocal(rs[:, :], rs[:, :]))
    chain.link(nc.vector.tensor_tensor(out=t, in0=rs[:, :], in1=rs[:, :], op=ALU.mult))
    chain.link(nc.vector.tensor_tensor(out=t, in0=t, in1=ve, op=ALU.mult))
    chain.link(nc.vector.tensor_scalar(out=t, in0=t, scalar1=-0.5, scalar2=1.5, op0=ALU.mult, op1=ALU.add))
    chain.link(nc.vector.tensor_tensor(out=rs[:, :], in0=rs[:, :], in1=t, op=ALU.mult))


def normalise(nc, x, y, mv, rs):
    for j in range(TC):
        last = nc.vector.tensor_scalar(out=y[:, j, 0:D], in0=x[:, j, :], scalar1=mv[:, j, 0:1], scalar2=rs[:, j:j + 1],
                                       op0=ALU.subtract, op1=ALU.mult)
    return last


def statistics(nc, chain, x, st, mv, passed):
    for j in range(TC):
        last = nc.vector.bn_stats(out=st[:, j, :], in_=x[:, j, :])
    chain.link(last, passed)
    for j in range(TC):
        last = nc.vector.bn_aggr(out=mv[:, j, :], in_=st[:, j, :])
    chain.link(last)


def in_two_stages(engine, NC, a, b, both=None):
    if both is None:
        def both(c1, s1, c, s):
            a(c1, s1)
            b(c, s)
    a(0, 0)
    with engine.Fori(0, NC // 2 - 1) as i:
        for s in range(2):
            both(i * 2 + s + 1, 1 - s, i * 2 + s, s)
    both(NC - 1, 1, NC - 2, 0)
    b(NC - 1, 1)


def positions(nc, B, S, x_d, idx):
    NT = B * S // P
    with ExitStack() as ctx:
        sb = lambda name, shape, dt: ctx.enter_context(nc.sbuf_tensor(name, shape, dt))
        sem = lambda name: ctx.enter_context(nc.semaphore(name))
        ids = sb("ids", [B, S], I32)
        start = sb("start", [B, S], F32)
        pos = sb("pos", [B, S], F32)
        row = sb("row", [B, 2, S], F32)
        by_tile_i = sb("by_tile_i", [NT, P], I32)
        by_tile = sb("by_tile", [NT, 3, P], F32)
        ident = sb("identp", [P, P], F32)
        cols = ctx.enter_context(nc.psum_tensor("cols", [P, 3, NT], F32))
        loaded, made, iota_done, step, rows_done, moved, tiled, turned = (
            sem(n) for n in ("ids_loaded", "identp_made", "pos_made", "pos_step", "rows_done", "rows_moved",
                             "ids_tiled", "idx_turned"))
        with nc.Block() as block:
            @block.sync
            def _(sp):
                sp.dma_start(ids[:, :], x_d).then_inc(loaded, 16)
                sp.dma_start(by_tile_i[:, :], x_d.rearrange("b (t p) -> (b t) p", p=P)).then_inc(loaded, 16)
                sp.wait_ge(rows_done, 1)
                for b in range(B):
                    for a in range(2):
                        sp.dma_start(by_tile[b * (S // P):(b + 1) * (S // P), 1 + a, :],
                                     row[b:b + 1, a, :].rearrange("b (t p) -> b t p", p=P)).then_inc(moved, 16)

            @block.gpsimd
            def _(pool):
                nc.gpsimd.iota(pos[:, :], pattern=[[1, S]], base=0, channel_multiplier=0,
                               allow_small_or_imprecise_dtypes=True).then_inc(iota_done, 1)
                make_identity(nc, pool, ident, made)

            @block.vector
            def _(dve):
                chain = Chain(dve, step)
                dve.wait_ge(loaded, 32)
                nc.vector.tensor_copy(by_tile[:, 0, :], by_tile_i[:, :]).then_inc(tiled, 1)
                nc.vector.memset(start[:, 0:1], 0.0)
                chain.link(nc.vector.tensor_scalar(out=start[:, 1:S], in0=ids[:, 0:S - 1], scalar1=float(NEXT_TOKEN),
                                                   scalar2=None, op0=ALU.is_equal))
                dve.wait_ge(iota_done, 1)
                nc.vector.tensor_tensor_scan(out=row[:, 0, :], data0=start[:, :], data1=start[:, :], initial=0.0,
                                             op0=ALU.add, op1=ALU.max)
                chain.link(nc.vector.tensor_tensor(out=start[:, :], in0=start[:, :], in1=pos[:, :], op=ALU.mult))
                chain.link(nc.vector.tensor_tensor_scan(out=row[:, 1, :], data0=start[:, :], data1=start[:, :],
                                                        initial=0.0, op0=ALU.max, op1=ALU.max))
                nc.vector.tensor_tensor(out=row[:, 1, :], in0=pos[:, :], in1=row[:, 1, :],
                                        op=ALU.subtract).then_inc(rows_done, 1)
                dve.wait_ge(turned, 1)
                nc.vector.tensor_copy(idx[:, :, :], cols[:, :, :]).then_inc(step, 1)

            @block.tensor
            def _(pe):
                pe.wait_ge(made, 2)
                pe.wait_ge(tiled, 1)
                pe.wait_ge(moved, 16 * 2 * B)
                for a in range(3):
                    last = nc.tensor.transpose(cols[:, a, :], by_tile[:, a, :], ident[0:NT, 0:NT])
                last.then_inc(turned, 1)


def embed_and_project(nc, NT, tables, norm_w, norm_b, wqkv, b_qkv, idx, h_d, qk_d, v_all):
    NC = NT // TC
    QK = 2 * D // P
    with ExitStack() as ctx:
        sb = lambda name, shape, dt: ctx.enter_context(nc.sbuf_tensor(name, shape, dt))
        pb = lambda name, shape, dt: ctx.enter_context(nc.psum_tensor(name, shape, dt))
        sem = lambda name: ctx.enter_context(nc.semaphore(name))
        w1 = sb("wqkv1", [P, 3 * D], F32)
        w2 = sb("wqkv2", [D2 + 1, 3 * D], F32)
        nw = sb("nw", [P, D], F32)
        nb = sb("nb", [P, D], F32)
        ident = sb("ident1", [P, P], F32)
        cur = sb("cur", [P, 2, 3, TC], I32)
        emb = sb("emb", [P, 2, 3, TC, D], F32)
        h = sb("h", [P, 2, TC, D], F32)
        xn = sb("xn", [P, 2, TC, D], F32)
        st = sb("st1", [P, TC, 6], F32)
        mv = sb("mv1", [P, TC, 2], F32)
        rs = sb("rs1", [P, TC], F32)
        tmp = sb("tmp1", [P, 2, TC], F32)
        x1 = sb("x1", [P, 2, CH], F32)
        x2 = sb("x2", [D2 + 1, 2, CH], F32)
        rest = sb("rest", [P, QK, CH], F32)
        parts = sb("parts", [P, 2, QK, 3, CH], BF16)
        t1 = pb("t1", [P, CH], F32)
        t2 = pb("t2", [D2, CH], F32)
        pq = [pb(f"pq{m}", [P, CH], F32) for m in range(QK)]
        pv = [pb(f"pv{m}", [P, CH], F32) for m in range(2)]
        (w_loaded, made, ones_set, cur_ready, emb_free, step, h_ready, var_ready, root_ready,
         xn_ready, turned, x_ready, qk_ready, hi_ready, rest_ready, mid_ready, low_ready, v_ready, v_done,
         passed) = (
            sem(n) for n in ("w_loaded made1 ones_set cur_ready emb_free step1 h_ready var1 root1 "
                             "xn_ready turned1 x_ready qk_ready hi_ready rest_ready mid_ready low_ready v_ready "
                             "v_done passed1").split())
        gathered, h_stored, parts_stored = ([sem(f"{n}{s}") for s in range(2)] for n in
                                            ("gathered", "h_stored", "parts_stored"))
        NG = 3 * TC * 16
        with nc.Block() as block:
            @block.gpsimd
            def _(pool):
                make_identity(nc, pool, ident, made)
                with nc.gpsimd.Fori(0, NC // 2) as i:
                    for s in range(2):
                        c = i * 2 + s
                        pool.wait_ge(emb_free, c + 1)
                        nc.gpsimd.tensor_copy(cur[:, s, :, :], idx[:, :, bass.ds(c * TC, TC)]).then_inc(cur_ready, 1)
                        pool.wait_ge(cur_ready, c + 1)
                        hold(pool, passed)
                        for a in range(3):
                            for j in range(TC):
                                nc.gpsimd.indirect_dma_start(
                                    out=emb[:, s, a, j, :], out_offset=None, in_=tables[a],
                                    in_offset=bass.IndirectOffsetOnAxis(ap=cur[:, s, a, j:j + 1], axis=0),
                                ).then_inc(gathered[s], 16)

            @block.sync
            def _(sp):
                sp.dma_start(w1[:, :], wqkv[0:P, :]).then_inc(w_loaded, 16)
                sp.dma_start(w2[0:D2, :], wqkv[P:D, :]).then_inc(w_loaded, 16)
                sp.dma_start(w2[D2:D2 + 1, :], b_qkv.rearrange("(a n) -> a n", a=1)).then_inc(w_loaded, 16)
                sp.dma_start(nw[:, :], norm_w.rearrange("(a n) -> a n", a=1).broadcast_to([P, D])).then_inc(w_loaded, 16)
                sp.dma_start(nb[:, :], norm_b.rearrange("(a n) -> a n", a=1).broadcast_to([P, D])).then_inc(w_loaded, 16)
                for s in range(2):
                    sp.sem_inc(h_stored[s], 16)
                    sp.sem_inc(parts_stored[s], 16 * QK)

                def a(c, s):
                    sp.wait_ge(h_ready, c + 1)
                    hold(sp, passed)
                    sp.dma_start(h_d[bass.ds(c * CH, CH), :].rearrange("(j p) d -> p j d", p=P),
                                 h[:, s, :, :]).then_inc(h_stored[s], 16)

                def b(c, s):
                    sp.wait_ge(low_ready, c + 1)
                    hold(sp, passed)
                    for m in range(QK):
                        sp.dma_start(qk_d[:, m * P:(m + 1) * P, bass.ds(c * CH, CH)].rearrange("s p n -> p s n"),
                                     parts[:, s, m, :, :]).then_inc(parts_stored[s], 16)

                in_two_stages(nc.sync, NC, a, b)
                for s in range(2):
                    sp.wait_ge(h_stored[s], 16 * (NC // 2 + 1))
                    sp.wait_ge(parts_stored[s], 16 * QK * (NC // 2 + 1))

            @block.vector
            def _(dve):
                nc.vector.memset(x2[D2:D2 + 1, :, :], 1.0).then_inc(ones_set, 1)
                dve.sem_inc(emb_free, 2)
                dve.wait_ge(w_loaded, 80)
                LINKS = 16

                def a(c, s):
                    chain = Chain(dve, step, c * LINKS)
                    hs, xs, es = h[:, s, :, :], xn[:, s, :, :], emb[:, s, :, :, :]
                    dve.wait_ge(gathered[s], (c - s) * (NG // 2) + NG)
                    for n in (1, 2):
                        chain.link(nc.vector.tensor_tensor(out=es[:, 0, :, :], in0=es[:, 0, :, :], in1=es[:, n, :, :],
                                                           op=ALU.add))
                    statistics(nc, chain, es[:, 0, :, :], st, mv, passed)

                    def weigh():
                        for j in range(TC):
                            last = nc.vector.scalar_tensor_tensor(out=xn[:, s, j, :], in0=es[:, 0, j, :],
                                                                  scalar=mv[:, j, 0:1], in1=nw[:, :],
                                                                  op0=ALU.subtract, op1=ALU.mult)
                        last.then_inc(emb_free, 1)

                    inverse_std(nc, dve, chain, mv, EPS_TOK, rs, tmp, var_ready, root_ready, 2 * c + 1, weigh)
                    dve.wait_ge(h_stored[s], (c - s) * 8 + 16)
                    for j in range(TC):
                        last = nc.vector.scalar_tensor_tensor(out=h[:, s, j, :], in0=xn[:, s, j, :],
                                                              scalar=rs[:, j:j + 1], in1=nb[:, :], op0=ALU.mult,
                                                              op1=ALU.add)
                    last.then_inc(h_ready, 1)
                    dve.wait_ge(h_ready, c + 1)
                    statistics(nc, chain, hs, st, mv, passed)
                    inverse_std(nc, dve, chain, mv, EPS_LN, rs, tmp, var_ready, root_ready, 2 * c + 2)
                    normalise(nc, hs, xs, mv, rs).then_inc(xn_ready, 1)
                    assert chain.n == LINKS, chain.n

                def b(c, s):
                    for m in range(QK):
                        dve.wait_ge(hi_ready, c * QK + m + 1)
                        nc.vector.tensor_tensor(out=rest[:, m, :], in0=pq[m][:, :], in1=parts[:, s, m, 0, :],
                                                op=ALU.subtract).then_inc(rest_ready, 1)
                    for m in range(QK):
                        dve.wait_ge(mid_ready, c * QK + m + 1)
                        low = nc.vector.tensor_tensor(out=parts[:, s, m, 2, :], in0=rest[:, m, :],
                                                      in1=parts[:, s, m, 1, :], op=ALU.subtract)
                    low.then_inc(low_ready, 1)
                    dve.wait_ge(low_ready, c + 1)

                in_two_stages(nc.vector, NC, a, b)

            @block.scalar
            def _(act):
                act.sem_inc(x_ready, 1)
                act.sem_inc(rest_ready, QK)
                act.sem_inc(v_done, 1)

                def root(c, n):
                    act.wait_ge(var_ready, 2 * c + n + 1)
                    nc.scalar.activation(rs[:, :], tmp[:, 0, :], ACT.Sqrt).then_inc(root_ready, 1)

                def columns(c, s):
                    act.wait_ge(turned, c + 1)
                    nc.scalar.activation(x1[:, s, :], t1[:, :], ACT.Copy)
                    nc.scalar.activation(x2[0:D2, s, :], t2[:, :], ACT.Copy).then_inc(x_ready, 1)

                def high(c, s, m):
                    if m == 0:
                        act.wait_ge(parts_stored[s], (c - s) * (8 * QK) + 16 * QK)
                    act.wait_ge(qk_ready, c * QK + m + 1)
                    nc.scalar.activation(parts[:, s, m, 0, :], pq[m][:, :], ACT.Copy).then_inc(hi_ready, 1)

                def middle_and_values(c, s):
                    for m in range(QK):
                        act.wait_ge(rest_ready, (c + 1) * QK + m + 1)
                        nc.scalar.activation(parts[:, s, m, 1, :], rest[:, m, :], ACT.Copy).then_inc(mid_ready, 1)
                    act.wait_ge(v_ready, c + 1)
                    for m in range(2):
                        last = nc.scalar.activation(v_all[:, bass.ds(c * TC + 2 * m, 2), :],
                                                    pv[m][:, 0:2 * D].rearrange("p (j d) -> p j d", d=D), ACT.Copy)
                    last.then_inc(v_done, 1)

                def a(c, s):
                    for n in range(2):
                        root(c, n)

                def b(c, s):
                    columns(c, s)
                    for m in range(QK):
                        high(c, s, m)
                    middle_and_values(c, s)

                def both(c1, s1, c, s):
                    columns(c, s)
                    high(c, s, 0)
                    root(c1, 0)
                    high(c, s, 1)
                    root(c1, 1)
                    high(c, s, 2)
                    middle_and_values(c, s)

                assert QK == 3
                in_two_stages(nc.scalar, NC, a, b, both)

            @block.tensor
            def _(pe):
                pe.wait_ge(made, 2)
                pe.wait_ge(ones_set, 1)
                pe.wait_ge(w_loaded, 80)
                with nc.tensor.Fori(0, NC // 2) as i:
                    for s in range(2):
                        c = i * 2 + s
                        pe.wait_ge(xn_ready, c + 1)
                        pe.wait_ge(x_ready, c + 1)
                        for j in range(TC):
                            nc.tensor.transpose(t1[:, j * P:(j + 1) * P], xn[:, s, j, 0:P], ident[:, :])
                        for j in range(TC):
                            last = nc.tensor.transpose(t2[:, j * P:(j + 1) * P], xn[:, s, j, P:D], ident[:, :])
                        last.then_inc(turned, 1)
                        pe.wait_ge(x_ready, c + 2)
                        for m in range(QK):
                            pe.wait_ge(rest_ready, c * QK + QK)
                            nc.tensor.matmul(pq[m][:, :], w1[:, m * P:(m + 1) * P], x1[:, s, :], start=True, stop=False)
                            nc.tensor.matmul(pq[m][:, :], w2[:, m * P:(m + 1) * P], x2[:, s, :], start=False,
                                             stop=True).then_inc(qk_ready, 1)
                        pe.wait_ge(v_done, c + 1)
                        for j in range(TC):
                            o = pv[j // 2][:, (j % 2) * D:(j % 2 + 1) * D]
                            nc.tensor.matmul(o, x1[:, s, j * P:(j + 1) * P], w1[:, 2 * D:3 * D], start=True, stop=False)
                            last = nc.tensor.matmul(o, x2[:, s, j * P:(j + 1) * P], w2[:, 2 * D:3 * D], start=False,
                                                    stop=True)
                        last.then_inc(v_ready, 1)


def attention(nc, B, S, qk_d, v_all, attn):
    ST = S // P
    NQ = S // CH
    TRI = 3
    NL = B * HEADS // TRI
    PER = HEADS // TRI
    LEAD = ST + 4
    LAG = 2
    ROT = 4
    GS = TRI * ST
    RING = 3
    assert NQ == 4 and HEADS % TRI == 0 and GS % (LAG + 1) == 0 and GS * NQ % RING == 0 and NL > 1
    SCALE = float(HD) ** -0.5
    with ExitStack() as ctx:
        sb = lambda name, shape, dt: ctx.enter_context(nc.sbuf_tensor(name, shape, dt))
        pb = lambda name, shape, dt: ctx.enter_context(nc.psum_tensor(name, shape, dt))
        sem = lambda name: ctx.enter_context(nc.semaphore(name))
        q = [sb(f"q{n}", [SM, S], BF16) for n in range(TRI)]
        k = [sb(f"k{n}", [SM, S], BF16) for n in range(TRI)]
        v = [sb(f"v{n}", [P, ST, VW], F32) for n in range(TRI)]
        e = [sb(f"e{n}", [P, S], F32) for n in range(LAG + 1)]
        o = sb("o", [P, CH], F32)
        ident = sb("ident2", [P, P], F32)
        mx = sb("mx", [P, ST, NQ], F32)
        neg = sb("neg", [P, ST], F32)
        shift = sb("shift", [ST, 2, P], BF16)
        rd = sb("rd", [P, ST], F32)
        ps = [pb(f"ps{n}", [P, CH], F32) for n in range(RING)]
        pm = [pb(f"pm{n}", [P, CH], F32) for n in range(RING)]
        po = pb("po", [P, CH], F32)
        px = pb("px", [P, CH], F32)
        (made, consts, scored, row_ready, turned, turned_read, high_done, shift_ready, s_ready, e_ready,
         v_ready, pv_done, o_copied, o_turned, rd_done, passed) = (
            sem(n) for n in ("made2 consts2 scored row_ready turned2 turned_read high_done shift_ready s_ready "
                             "e_ready v_ready2 pv_done o_copied o_turned rd_done passed2").split())
        loaded = [sem(f"loaded{n}") for n in range(TRI)]
        maxed = [sem(f"maxed{n}") for n in range(RING)]
        shifted = [sem(f"shifted{n}") for n in range(TRI)]

        def run(engine, step):
            for i in range(ROT):
                step(0, 0, i)

            def body(t, last):
                for j in range(TRI):
                    for i in range(ROT, ST):
                        step(t, j, i)
                    if not (last and j == TRI - 1):
                        for i in range(ROT):
                            step(t + (j + 1) // TRI, (j + 1) % TRI, i)

            with engine.Fori(0, NL - 1) as t:
                body(t, False)
            body(NL - 1, True)

        def has_max(T, j, i):
            return not (isinstance(T, int) and T == NL - 1 and j * ST + i + LEAD >= GS)

        with nc.Block() as block:
            @block.sync
            def _(sp):
                def load(T, j):
                    cols = bass.ds((T // PER) * S, S)
                    ch = (T % PER) * (TRI * HD) + j * HD
                    row = 0
                    for part, n in ((0, 3), (1, 2), (2, 1)):
                        rows = slice(row, row + n * HD)
                        sp.dma_start(q[j][rows, :], qk_d[part:part + 1, bass.ds(ch, HD), cols].broadcast_to(
                            [n, HD, S])).then_inc(loaded[j], 16)
                        sp.dma_start(k[j][rows, :], qk_d[0:n, bass.ds(ch + D, HD), cols]).then_inc(loaded[j], 16)
                        row += n * HD

                def send_shift(T, j):
                    sp.wait_ge(shift_ready, T * TRI + j + 1)
                    hold(sp, passed)
                    for r in range(2):
                        sp.dma_start(q[j][SK + r:SK + r + 1, :], shift[:, r, :]).then_inc(shifted[j], 16)

                for j in range(TRI):
                    load(0, j)
                send_shift(0, 0)
                with nc.sync.Fori(0, NL - 1) as t:
                    for j in range(TRI):
                        send_shift(t + (j + 1) // TRI, (j + 1) % TRI)
                        sp.wait_ge(s_ready, t * (GS * NQ) + (j + 1) * ST * NQ)
                        hold(sp, passed)
                        load(t + 1, j)
                for j in range(1, TRI):
                    send_shift(NL - 1, j)

            @block.gpsimd
            def _(pool):
                make_identity(nc, pool, ident, made)

                def fetch(T, j):
                    nc.gpsimd.tensor_copy(v[j][:, :, 0:HD],
                                          v_all[:, bass.ds((T // PER) * ST, ST),
                                                bass.ds((T % PER) * (TRI * HD) + j * HD, HD)]).then_inc(v_ready, 1)

                for j in range(TRI):
                    fetch(0, j)
                with nc.gpsimd.Fori(1, NL) as t:
                    for j in range(TRI):
                        pool.wait_ge(pv_done, t * GS + (j + 1) * ST - GS)
                        hold(pool, passed)
                        fetch(t, j)

            @block.tensor
            def _(pe):
                pe.wait_ge(made, 2)
                pe.wait_ge(consts, TRI)

                def max_tile(T, j, i, cs):
                    jj, im = divmod(j * ST + i + LEAD, ST)
                    Tm, jm = T + jj // TRI, jj % TRI
                    if im == 0 and cs[0] == 0:
                        pe.wait_ge(loaded[jm], (Tm + 1) * 96)
                    for c in cs:
                        n = (j * ST + i + LEAD) * NQ + c
                        if not (isinstance(T, int) and T * GS * NQ + n < RING):
                            pe.wait_ge(maxed[n % RING], T * (GS * NQ // RING) + n // RING)
                        nc.tensor.matmul(pm[n % RING][:, :], q[jm][0:SK, im * P:(im + 1) * P],
                                         k[jm][0:SK, c * CH:(c + 1) * CH], start=True, stop=True).then_inc(scored, 1)

                def scores(T, j, i, c):
                    n = (j * ST + i) * NQ + c
                    if i == 0 and c == 0:
                        pe.wait_ge(shifted[j], (T + 1) * 32)
                    if not (isinstance(T, int) and T == 0 and n < RING):
                        pe.wait_ge(e_ready, T * (GS * NQ) + n + 1 - RING)
                    nc.tensor.matmul(ps[n % RING][:, :], k[j][0:SM, i * P:(i + 1) * P],
                                     q[j][0:SM, c * CH:(c + 1) * CH], start=True, stop=True).then_inc(s_ready, 1)

                def values(T, j, i):
                    g = j * ST + i - LAG
                    jv, iv = (g // ST) % TRI, g % ST
                    pe.wait_ge(e_ready, T * (GS * NQ) + (g + 1) * NQ)
                    if iv == 0:
                        pe.wait_ge(v_ready, T * TRI + j + 1)
                        if not (isinstance(T, int) and T == 0 and j == 0):
                            pe.wait_ge(o_copied, T * TRI + j)
                    for c in range(NQ):
                        last = nc.tensor.matmul(po[32 * c:32 * c + VW, :], v[jv][:, iv, :],
                                                e[g % (LAG + 1)][:, c * CH:(c + 1) * CH],
                                                start=(iv == 0), stop=(iv == ST - 1))
                    last.then_inc(pv_done, 1)

                def turn_shift(H):
                    pe.wait_ge(row_ready, H + 1)
                    if not (isinstance(H, int) and H == 0):
                        pe.wait_ge(turned_read, 2 * H - 1)
                    nc.tensor.transpose(px[0:ST, 0:P], neg[:, :], ident[:, :]).then_inc(turned, 1)

                def turn_output(H):
                    pe.wait_ge(o_copied, H + 1)
                    pe.wait_ge(turned_read, 2 * H + (1 if isinstance(H, int) else 2))
                    for c in range(NQ):
                        last = nc.tensor.transpose(px[:, c * P:(c + 1) * P], o[:, c * P:(c + 1) * P], ident[:, :])
                    last.then_inc(o_turned, 1)

                def step(T, j, i):
                    m = has_max(T, j, i)
                    early = isinstance(T, int) and T == 0 and j == 0
                    if i == 13 and not (isinstance(T, int) and T == NL - 1 and j == TRI - 1):
                        turn_shift(T * TRI + j + 1)
                    for c in range(NQ):
                        if m:
                            max_tile(T, j, i, (c,))
                        scores(T, j, i, c)
                        if c == 1 and not (early and i < LAG):
                            values(T, j, i)
                    if i == 3 and not early:
                        turn_output(T * TRI + j - 1)

                for g in range(-LEAD, 0):
                    max_tile(0, 0, g, range(NQ))
                turn_shift(0)
                run(nc.tensor, step)
                for i in range(LAG):
                    values(NL, 0, i)
                turn_output(NL * TRI - 1)

            @block.scalar
            def _(act):
                def copy_output(H):
                    act.wait_ge(pv_done, (H + 1) * ST)
                    if not (isinstance(H, int) and H == 0):
                        act.wait_ge(o_turned, H)
                    nc.scalar.activation(o[:, :], po[:, :], ACT.Copy).then_inc(o_copied, 1)

                def step(T, j, i):
                    early = isinstance(T, int) and T == 0 and j == 0
                    g = j * ST + i
                    for c in range(NQ):
                        n = g * NQ + c
                        act.wait_ge(s_ready, T * (GS * NQ) + n + 1)
                        if c == 0 and not (early and i <= LAG):
                            act.wait_ge(pv_done, T * GS + g - LAG)
                        nc.scalar.activation(e[g % (LAG + 1)][:, c * CH:(c + 1) * CH], ps[n % RING][:, :],
                                             ACT.Exp, scale=SCALE).then_inc(e_ready, 1)
                        if i == 1 and c == 1 and not early:
                            copy_output(T * TRI + j - 1)

                run(nc.scalar, step)
                copy_output(NL * TRI - 1)

            @block.vector
            def _(dve):
                def maxima(T, j, i):
                    jj, im = divmod(j * ST + i + LEAD, ST)
                    for c in range(NQ):
                        n = (j * ST + i + LEAD) * NQ + c
                        dve.wait_ge(scored, T * (GS * NQ) + n + 1)
                        nc.vector.tensor_reduce(out=mx[:, im, c:c + 1], in_=pm[n % RING][:, :], op=ALU.max,
                                                axis=AX.X).then_inc(maxed[n % RING], 1)
                    if im == ST - 1:
                        dve.wait_ge(maxed[n % RING], T * (GS * NQ // RING) + n // RING + 1)
                        nc.vector.tensor_reduce(out=neg[:, :], in_=mx[:, :, :], op=ALU.max, axis=AX.X,
                                                negate=True).then_inc(row_ready, 1)
                        dve.wait_ge(row_ready, T * TRI + jj + 1)

                def split_shift(T, j):
                    H = T * TRI + j
                    dve.wait_ge(turned, H + 1)
                    if not (isinstance(H, int) and H == 0):
                        Tp, jp = (T, j - 1) if j else (T - 1, TRI - 1)
                        dve.wait_ge(shifted[jp], (Tp + 1) * 32)
                    nc.vector.tensor_copy(shift[:, 0, :], px[0:ST, 0:P]).then_inc(high_done, 1)
                    dve.wait_ge(high_done, H + 1)
                    nc.vector.tensor_tensor(out=shift[:, 1, :], in0=px[0:ST, 0:P], in1=shift[:, 0, :],
                                            op=ALU.subtract).then_inc(shift_ready, 1)
                    dve.wait_ge(shift_ready, H + 1)
                    dve.sem_inc(turned_read, 1)

                def normalise_output(T, j):
                    H = T * TRI + j
                    out = px[:, :].rearrange("p (c b w) -> p c b w", b=NQ, w=VW)
                    rdv = rd[:, :].rearrange("p (c b) -> p c b", b=NQ)
                    dve.wait_ge(o_turned, H + 1)
                    nc.vector.reciprocal(rdv, out[:, :, :, HD]).then_inc(rd_done, 1)
                    dve.wait_ge(rd_done, H + 1)
                    to = attn[:, bass.ds((T // PER) * ST, ST), bass.ds((T % PER) * (TRI * HD) + j * HD, HD)]
                    nc.vector.tensor_tensor(out=to.rearrange("p (b c) d -> p c b d", c=NQ), in0=out[:, :, :, 0:HD],
                                            in1=rdv.unsqueeze(3).broadcast_to([P, NQ, NQ, HD]),
                                            op=ALU.mult).then_inc(turned_read, 1)

                def step(T, j, i):
                    early = isinstance(T, int) and T == 0 and j == 0
                    if has_max(T, j, i):
                        maxima(T, j, i)
                    if i == 13 and not (isinstance(T, int) and T == NL - 1 and j == TRI - 1):
                        split_shift(T + (j + 1) // TRI, (j + 1) % TRI)
                    if i == 3 and not early:
                        normalise_output(T if j else T - 1, (j - 1) % TRI)

                for n in range(TRI):
                    nc.vector.memset(v[n][:, :, HD + 1:VW], 0.0)
                    nc.vector.memset(v[n][:, :, HD:HD + 1], 1.0)
                    nc.vector.memset(k[n][SK:SM, :], 1.0).then_inc(consts, 1)
                for g in range(-LEAD, 0):
                    maxima(0, 0, g)
                split_shift(0, 0)
                run(nc.vector, step)
                normalise_output(NL - 1, TRI - 1)


def project_and_gate(nc, NT, E, attn, w_out, b_out, gate, h_d, xs_d, xt_d, z_all):
    NC = NT // TC
    with ExitStack() as ctx:
        sb = lambda name, shape, dt: ctx.enter_context(nc.sbuf_tensor(name, shape, dt))
        pb = lambda name, shape, dt: ctx.enter_context(nc.psum_tensor(name, shape, dt))
        sem = lambda name: ctx.enter_context(nc.semaphore(name))
        w1 = sb("wo1", [P, D], F32)
        w2 = sb("wo2", [D2 + 1, D], F32)
        g1 = sb("gate1", [P, E], F32)
        g2 = sb("gate2", [D2, E], F32)
        ident = sb("ident3", [P, P], F32)
        ac = sb("ac", [P, 2, TC, D], F32)
        h = sb("h3", [P, 2, TC, D], F32)
        x = sb("x3", [P, 2, TC, D], F32)
        a1 = sb("a1", [P, CH], F32)
        a2 = sb("a2", [D2 + 1, CH], F32)
        x1 = sb("x31", [P, 2, CH], F32)
        x2 = sb("x32", [D2, 2, CH], F32)
        st = sb("st3", [P, TC, 6], F32)
        mv = sb("mv3", [P, TC, 2], F32)
        rs = sb("rs3", [P, TC], F32)
        tmp = sb("tmp3", [P, 2, TC], F32)
        ta1 = pb("ta1", [P, CH], F32)
        ta2 = pb("ta2", [D2, CH], F32)
        tx1 = pb("tx1", [P, CH], F32)
        tx2 = pb("tx2", [D2, CH], F32)
        pp = [pb(f"pp{m}", [P, 2, D], F32) for m in range(2)]
        pt = pb("pt", [P, TC, E], F32)
        (made, w_loaded, ones_set, ac_ready, a_turned, a_ready, projected, summed, var_ready, root_ready, step,
         x_ready, x_turned, columns_ready, z_ready, z_copied, passed) = (
            sem(n) for n in ("made3 w_loaded3 ones3 ac_ready a_turned a_ready projected summed var3 root3 "
                             "step3 x_ready3 x_turned columns_ready z_ready z_copied passed3").split())
        h_loaded, h_stored, x_stored, columns_stored = (
            [sem(f"{n}{s}") for s in range(2)] for n in ("h_loaded3", "h_stored3", "x_stored3", "columns_stored"))
        with nc.Block() as block:
            @block.sync
            def _(sp):
                for dst, src in ((w1[:, :], w_out[0:P, :]), (w2[0:D2, :], w_out[P:D, :]),
                                 (w2[D2:D2 + 1, :], b_out.rearrange("(a n) -> a n", a=1)),
                                 (g1[:, :], gate[0:P, :]), (g2[:, :], gate[P:D, :])):
                    sp.dma_start(dst, src).then_inc(w_loaded, 16)
                for s in range(2):
                    sp.sem_inc(h_stored[s], 16)
                    sp.sem_inc(x_stored[s], 16)
                    sp.sem_inc(columns_stored[s], 32)

                def a(c, s):
                    rows = bass.ds(c * CH, CH)
                    sp.wait_ge(summed, c + 2)
                    hold(sp, passed)
                    sp.dma_start(h_d[rows, :].rearrange("(j p) d -> p j d", p=P), h[:, s, :, :]).then_inc(h_stored[s], 16)
                    sp.wait_ge(x_ready, c + 3)
                    hold(sp, passed)
                    sp.dma_start(xs_d[rows, 0:D].rearrange("(j p) d -> p j d", p=P), x[:, s, :, :]).then_inc(
                        x_stored[s], 16)

                def b(c, s):
                    cols = bass.ds(c * CH, CH)
                    sp.wait_ge(columns_ready, c + 2)
                    hold(sp, passed)
                    sp.dma_start(xt_d[0:P, cols], x1[:, s, :]).then_inc(columns_stored[s], 16)
                    sp.dma_start(xt_d[P:D, cols], x2[:, s, :]).then_inc(columns_stored[s], 16)

                in_two_stages(nc.sync, NC, a, b)
                for s in range(2):
                    sp.wait_ge(h_stored[s], 16 * (NC // 2 + 1))
                    sp.wait_ge(x_stored[s], 16 * (NC // 2 + 1))
                    sp.wait_ge(columns_stored[s], 32 * (NC // 2 + 1))

            @block.gpsimd
            def _(pool):
                make_identity(nc, pool, ident, made)
                with nc.gpsimd.Fori(0, NC // 2) as i:
                    for s in range(2):
                        c = i * 2 + s
                        pool.wait_ge(a_turned, c + 1)
                        hold(pool, passed)
                        nc.gpsimd.tensor_copy(ac[:, s, :, :], attn[:, bass.ds(c * TC, TC), :]).then_inc(ac_ready, 1)
                        pool.wait_ge(h_stored[s], (i + 1) * 16)
                        pool.wait_ge(x_ready, c + 1)
                        hold(pool, passed)
                        nc.gpsimd.dma_start(h[:, s, :, :], h_d[bass.ds(c * CH, CH), :].rearrange(
                            "(j p) d -> p j d", p=P)).then_inc(h_loaded[s], 16)

            @block.tensor
            def _(pe):
                pe.wait_ge(made, 2)
                pe.wait_ge(w_loaded, 80)
                pe.wait_ge(ones_set, 1)
                pe.sem_inc(a_turned, 2)
                pe.sem_inc(x_turned, 2)

                def turn_a(c, s):
                    pe.wait_ge(ac_ready, c + 1)
                    pe.wait_ge(a_ready, c + 1)
                    for j in range(TC):
                        nc.tensor.transpose(ta1[:, j * P:(j + 1) * P], ac[:, s, j, 0:P], ident[:, :])
                    for j in range(TC):
                        last = nc.tensor.transpose(ta2[:, j * P:(j + 1) * P], ac[:, s, j, P:D], ident[:, :])
                    last.then_inc(a_turned, 1)

                def project(c, s):
                    pe.wait_ge(a_ready, c + 2)
                    pe.wait_ge(summed, c + 1)
                    for j in range(TC):
                        out = pp[j // 2][:, j % 2, :]
                        nc.tensor.matmul(out, a1[:, j * P:(j + 1) * P], w1[:, :], start=True, stop=False)
                        last = nc.tensor.matmul(out, a2[:, j * P:(j + 1) * P], w2[:, :], start=False, stop=True)
                    last.then_inc(projected, 1)

                def turn_x(c, s):
                    pe.wait_ge(x_ready, c + 3)
                    pe.wait_ge(columns_ready, c + 1)
                    for j in range(TC):
                        nc.tensor.transpose(tx1[:, j * P:(j + 1) * P], x[:, s, j, :][:, 0:P], ident[:, :])
                    for j in range(TC):
                        last = nc.tensor.transpose(tx2[:, j * P:(j + 1) * P], x[:, s, j, :][:, P:D], ident[:, :])
                    last.then_inc(x_turned, 1)

                def logits(c, s):
                    pe.wait_ge(columns_ready, c + 2)
                    pe.wait_ge(z_copied, c + 1)
                    for j in range(TC):
                        nc.tensor.matmul(pt[:, j, :], x1[:, s, j * P:(j + 1) * P], g1[:, :], start=True, stop=False)
                        last = nc.tensor.matmul(pt[:, j, :], x2[:, s, j * P:(j + 1) * P], g2[:, :], start=False,
                                                stop=True)
                    last.then_inc(z_ready, 1)

                def both(c1, s1, c, s):
                    project(c1, s1)
                    turn_x(c, s)
                    if not (isinstance(c, int) and c1 == NC - 1):
                        turn_a(c1 + 1, s)
                    logits(c, s)

                def a(c, s):
                    turn_a(c, s)
                    project(c, s)
                    turn_a(c + 1, 1 - s)

                def b(c, s):
                    turn_x(c, s)
                    logits(c, s)

                in_two_stages(nc.tensor, NC, a, b, both)

            @block.scalar
            def _(act):
                act.sem_inc(a_ready, 1)
                act.sem_inc(columns_ready, 1)
                act.sem_inc(z_copied, 1)

                def move_a(c):
                    act.wait_ge(a_turned, c + 3)
                    act.wait_ge(projected, c + 1)
                    nc.scalar.activation(a1[:, :], ta1[:, :], ACT.Copy)
                    nc.scalar.activation(a2[0:D2, :], ta2[:, :], ACT.Copy).then_inc(a_ready, 1)

                def root(c):
                    act.wait_ge(var_ready, c + 1)
                    nc.scalar.activation(rs[:, :], tmp[:, 0, :], ACT.Sqrt).then_inc(root_ready, 1)

                def move_x(c, s):
                    act.wait_ge(x_turned, c + 3)
                    act.wait_ge(columns_stored[s], (c - s) * 16 + 32)
                    nc.scalar.activation(x1[:, s, :], tx1[:, :], ACT.Copy)
                    nc.scalar.activation(x2[:, s, :], tx2[:, :], ACT.Copy).then_inc(columns_ready, 1)

                def move_z(c):
                    act.wait_ge(z_ready, c + 1)
                    nc.scalar.activation(z_all[:, bass.ds(c * TC, TC), :], pt[:, :, :], ACT.Copy).then_inc(z_copied, 1)

                def both(c1, s1, c, s):
                    move_x(c, s)
                    if not (isinstance(c, int) and c1 == NC - 1):
                        move_a(c1 + 1)
                    root(c1)
                    move_z(c)

                def a(c, s):
                    move_a(c)
                    move_a(c + 1)
                    root(c)

                def b(c, s):
                    move_x(c, s)
                    move_z(c)

                in_two_stages(nc.scalar, NC, a, b, both)

            @block.vector
            def _(dve):
                nc.vector.memset(a2[D2:D2 + 1, :], 1.0).then_inc(ones_set, 1)
                dve.sem_inc(projected, 1)
                dve.sem_inc(summed, 1)
                dve.sem_inc(x_ready, 2)
                LINKS = 7

                def a(c, s):
                    chain = Chain(dve, step, c * LINKS)
                    dve.wait_ge(projected, c + 2)
                    dve.wait_ge(h_loaded[s], (c - s) * 8 + 16)
                    for m in range(2):
                        last = nc.vector.tensor_tensor(out=h[:, s, 2 * m:2 * m + 2, :], in0=pp[m][:, :, :],
                                                       in1=h[:, s, 2 * m:2 * m + 2, :], op=ALU.add)
                    last.then_inc(summed, 1)
                    dve.wait_ge(summed, c + 2)
                    statistics(nc, chain, h[:, s, :, :], st, mv, passed)
                    inverse_std(nc, dve, chain, mv, EPS_LN, rs, tmp, var_ready, root_ready, c + 1)
                    dve.wait_ge(x_stored[s], (c - s) * 8 + 16)
                    dve.wait_ge(x_turned, c + 1)
                    normalise(nc, h[:, s, :, :], x[:, s, :, :], mv, rs).then_inc(x_ready, 1)
                    assert chain.n == LINKS, chain.n

                in_two_stages(nc.vector, NC, a, lambda c, s: None)


def shared_and_choose(nc, NT, E, CAP, ws_g, ws_u, ws_d, h_d, xs_d, xt_d, z_all, out, c_d, ct_d):
    NC = NT // TC
    SEG = P // E
    L = NT * P // SEG
    FS = ws_d.shape[0] // P
    ROUNDS = 32
    PER = ROUNDS // NC
    assert PER * NC == ROUNDS
    with ExitStack() as ctx:
        sb = lambda name, shape, dt: ctx.enter_context(nc.sbuf_tensor(name, shape, dt))
        pb = lambda name, shape, dt: ctx.enter_context(nc.psum_tensor(name, shape, dt))
        sem = lambda name: ctx.enter_context(nc.semaphore(name))
        wg1 = sb("wsg1", [P, FS * P], F32)
        wg2 = sb("wsg2", [D2, FS * P], F32)
        wu1 = sb("wsu1", [P, FS * P], F32)
        wu2 = sb("wsu2", [D2, FS * P], F32)
        wd = sb("wsd", [P, FS, D], F32)
        score = sb("score", [P, NT, E], F32)
        x1 = sb("x41", [P, 2, CH], F32)
        x2 = sb("x42", [D2, 2, CH], F32)
        h = sb("h4", [P, 2, TC, D], F32)
        sg = sb("sg4", [P, 2, CH], F32)
        act_sb = sb("act4", [P, 2, FS, CH], F32)
        zp = sb("zp", [P, L // P, E, SEG], F32)
        z = sb("z4", [P, L], F32)
        gt = sb("gt", [P, L], F32)
        eq = sb("eq", [P, L], F32)
        rank = sb("rank", [P, L], F32)
        ident = sb("ident4", [P, P], F32)
        same = sb("same", [P, P], F32)
        before = sb("before", [P, P], F32)
        prefix = sb("prefix", [P, 1], I32)
        bit = sb("bit", [P, 1], I32)
        cand = sb("cand", [P, 1], I32)
        sign = sb("sign", [P, 1], I32)
        key = sb("key", [P, 1], I32)
        cnt = sb("cnt", [P, 2], F32)
        few = sb("few", [P, 1], F32)
        ct = sb("ct", [P, L // P], F32)
        pg = [pb(f"pg{m}", [P, CH], F32) for m in range(2)]
        pu = [pb(f"pu{m}", [P, CH], F32) for m in range(2)]
        pd = [pb(f"pd{m}", [P, 2, D], F32) for m in range(2)]
        pc = pb("pc", [P, 2], F32)
        (w_loaded, z_ordered, z_turned, z_ready, made, score_ready, u_ready, g_ready, silu_ready, gated, down_ready, sum_ready, counted,
         totalled, step, passed, c_ready, all_stored) = (
            sem(n) for n in ("w_loaded4 z_ordered z_turned z_ready4 made4 score_ready u_ready g_ready silu_ready gated down_ready "
                             "sum_ready counted totalled step4 passed4 c_ready all_stored").split())
        x_loaded, h_loaded, h_stored = ([sem(f"{n}{s}") for s in range(2)] for n in
                                        ("x_loaded4", "h_loaded4", "h_stored4"))
        with nc.Block() as block:
            @block.sync
            def _(sp):
                for dst, src in ((wg1[:, :], ws_g[0:P, :]), (wg2[:, :], ws_g[P:D, :]), (wu1[:, :], ws_u[0:P, :]),
                                 (wu2[:, :], ws_u[P:D, :]), (wd[:, :, :], ws_d.rearrange("(f p) d -> p f d", p=P))):
                    sp.dma_start(dst, src).then_inc(w_loaded, 16)
                for s in range(2):
                    sp.sem_inc(h_stored[s], 16)

                def a(c, s):
                    cols = bass.ds(c * CH, CH)
                    sp.wait_ge(h_stored[s], (c - s) * 8 + 16)
                    hold(sp, passed)
                    sp.dma_start(h[:, s, :, :], h_d[cols, :].rearrange("(j p) d -> p j d", p=P)).then_inc(
                        h_loaded[s], 16)

                def b(c, s):
                    sp.wait_ge(sum_ready, c + 2)
                    hold(sp, passed)
                    sp.dma_start(out[bass.ds(c * CH, CH), :].rearrange("(j p) d -> p j d", p=P),
                                 h[:, s, :, :]).then_inc(h_stored[s], 16)

                in_two_stages(nc.sync, NC, a, b)
                for s in range(2):
                    sp.wait_ge(h_stored[s], 16 * (NC // 2 + 1))
                rows = c_d.rearrange("(e s l) -> e s l", s=SEG, l=L)
                tiles = ct_d.rearrange("(e s l) -> e s l", s=SEG, l=L // P)
                sp.wait_ge(c_ready, 1)
                sp.dma_start(rows[0:E, :, :].rearrange("e s l -> (e s) l"), rank[:, :]).then_inc(all_stored, 16)
                sp.dma_start(tiles[0:E, :, :].rearrange("e s l -> (e s) l"), ct[:, :]).then_inc(all_stored, 16)
                sp.dma_start(rows[E:E + AHEAD, :, :].rearrange("e s l -> (e s) l"), rank[0:AHEAD * SEG, :]).then_inc(
                    all_stored, 16)
                sp.dma_start(tiles[E:E + AHEAD, :, :].rearrange("e s l -> (e s) l"), ct[0:AHEAD * SEG, :]).then_inc(
                    all_stored, 16)
                sp.wait_ge(score_ready, 1)
                sp.dma_start(xs_d[:, D:D + E].rearrange("(t p) e -> p t e", p=P), score[:, :, :]).then_inc(all_stored, 16)
                sp.wait_ge(all_stored, 80)

            @block.gpsimd
            def _(pool):
                def select(m, base, pattern, cm, n):
                    nc.gpsimd.affine_select(out=m[:, :], in_=m[:, :], compare_op=ALU.is_ge, fill=0.0, base=base,
                                            pattern=pattern, channel_multiplier=cm).then_inc(made, 1)
                    pool.wait_ge(made, n)

                def load_x(c, s):
                    pool.wait_ge(u_ready, (c + 1) * FS)
                    hold(pool, passed)
                    cols = bass.ds(c * CH, CH)
                    nc.gpsimd.dma_start(x1[:, s, :], xt_d[0:P, cols]).then_inc(x_loaded[s], 16)
                    nc.gpsimd.dma_start(x2[:, s, :], xt_d[P:D, cols]).then_inc(x_loaded[s], 16)

                for s in range(2):
                    load_x(s, s)
                make_identity(nc, pool, ident, made)
                nc.gpsimd.memset(same[:, :], 1.0).then_inc(made, 1)
                pool.wait_ge(made, 3)
                select(same, 0, [[-SEG, E], [0, SEG]], 1, 4)
                select(same, SEG - 1, [[SEG, E], [0, SEG]], -1, 5)
                nc.gpsimd.tensor_copy(before[:, :], same[:, :]).then_inc(made, 1)
                pool.wait_ge(made, 6)
                select(before, -1, [[1, P]], -1, 7)
                with nc.gpsimd.Fori(1, NC // 2) as i:
                    for s in range(2):
                        load_x(i * 2 + s, s)

            @block.tensor
            def _(pe):
                pe.sem_inc(u_ready, 2 * FS)
                pe.wait_ge(made, 2)
                pe.wait_ge(z_ordered, 1)
                for u in range(L // P):
                    last = nc.tensor.transpose(pg[u // TC][:, (u % TC) * P:(u % TC + 1) * P],
                                               zp[:, u, :, :].rearrange("p e s -> p (e s)"), ident[:, :])
                last.then_inc(z_turned, 1)
                pe.wait_ge(w_loaded, 80)
                pe.wait_ge(made, 7)
                pe.wait_ge(z_ready, 1)

                def total(n):
                    pe.wait_ge(counted, n + 1)
                    nc.tensor.matmul(pc[:, 0:1], same[:, :], cnt[:, 0:1], start=True, stop=True).then_inc(totalled, 1)

                def a(c, s):
                    pe.wait_ge(x_loaded[s], (c - s) * 16 + 32)
                    for f in range(FS):
                        pe.wait_ge(gated, c * FS + f + 1)
                        fs = slice(f * P, (f + 1) * P)
                        for w1, w2, o, done in ((wg1, wg2, pg, g_ready), (wu1, wu2, pu, u_ready)):
                            t = o[(s * FS + f) % 2]
                            nc.tensor.matmul(t[:, :], w1[:, fs], x1[:, s, :], start=True, stop=False)
                            nc.tensor.matmul(t[:, :], w2[:, fs], x2[:, s, :], start=False, stop=True).then_inc(done, 1)
                        for r in range(PER):
                            if r * FS // PER == f:
                                total(c * PER + r)

                def b(c, s):
                    pe.wait_ge(gated, (c + 1) * FS + 2)
                    pe.wait_ge(sum_ready, c + 1)
                    for j in range(TC):
                        for f in range(FS):
                            last = nc.tensor.matmul(pd[j // 2][:, j % 2, :], act_sb[:, s, f, j * P:(j + 1) * P],
                                                    wd[:, f, :], start=(f == 0), stop=(f == FS - 1))
                    last.then_inc(down_ready, 1)

                in_two_stages(nc.tensor, NC, a, b)
                pe.wait_ge(counted, ROUNDS + 1)
                nc.tensor.matmul(pc[:, 0:1], same[:, :], cnt[:, 0:1], start=True, stop=True)
                nc.tensor.matmul(pc[:, 1:2], before[:, :], cnt[:, 1:2], start=True, stop=True).then_inc(totalled, 1)
                pe.wait_ge(counted, ROUNDS + 2)
                nc.tensor.matmul(pc[:, 0:1], before[:, :], cnt[:, 0:1], start=True, stop=True).then_inc(totalled, 1)

            @block.scalar
            def _(act):
                act.wait_ge(z_turned, 1)
                for u in range(0, L, CH):
                    last = nc.scalar.activation(z[:, u:min(u + CH, L)], pg[u // CH][:, 0:min(CH, L - u)], ACT.Copy)
                last.then_inc(z_ready, 1)
                nc.scalar.activation(score[:, :, :], z_all[:, :, :], ACT.Sigmoid).then_inc(score_ready, 1)

                def a(c, s):
                    for f in range(FS):
                        act.wait_ge(g_ready, c * FS + f + 1)
                        act.wait_ge(gated, c * FS + f + 1)
                        nc.scalar.activation(sg[:, (s * FS + f) % 2, :], pg[(s * FS + f) % 2][:, :],
                                             ACT.Silu).then_inc(silu_ready, 1)

                in_two_stages(nc.scalar, NC, a, lambda c, s: None)

            @block.vector
            def _(dve):
                dve.sem_inc(gated, 2)
                dve.sem_inc(sum_ready, 1)
                nc.vector.tensor_copy(zp[:, :, :, :], z_all[:, :, :].rearrange("p (s u) e -> p u e s", s=SEG)).then_inc(
                    z_ordered, 1)
                chain = Chain(dve, step)
                nc.vector.memset(prefix[:, :], 0)
                nc.vector.memset(bit[:, :], -2**31)
                chain.link(nc.vector.memset(few[:, :], float(CAP)))
                dve.wait_ge(z_ready, 1)
                LINKS = 7
                FIRST = 4
                first = chain.n

                def as_logit(chain, k):
                    chain.link(nc.vector.tensor_single_scalar(out=sign[:, :], in_=k, scalar=31,
                                                              op=ALU.arith_shift_right))
                    chain.link(nc.vector.tensor_scalar(out=sign[:, :], in0=sign[:, :], scalar1=-1, scalar2=-2**31,
                                                       op0=ALU.bitwise_xor, op1=ALU.bitwise_or))
                    chain.link(nc.vector.tensor_tensor(out=key[:, :], in0=k, in1=sign[:, :], op=ALU.bitwise_xor))

                def ask(n):
                    chain = Chain(dve, step, first + n * LINKS)
                    chain.link(nc.vector.tensor_tensor(out=cand[:, :], in0=prefix[:, :], in1=bit[:, :],
                                                       op=ALU.bitwise_or))
                    as_logit(chain, cand[:, :])
                    nc.vector.tensor_scalar(out=gt[:, :], in0=z[:, :], scalar1=key[:, :].bitcast(F32), scalar2=None,
                                            op0=ALU.is_ge, op1=ALU.add, accum_out=cnt[:, 0:1]).then_inc(counted, 1)
                    assert chain.n == FIRST

                def answer(n):
                    chain = Chain(dve, step, first + n * LINKS + FIRST)
                    dve.wait_ge(totalled, n + 1)
                    chain.link(nc.vector.tensor_scalar(out=sign[:, :], in0=pc[:, 0:1], scalar1=float(CAP),
                                                       scalar2=-1.0, op0=ALU.is_ge, op1=ALU.mult))
                    chain.link(nc.vector.tensor_tensor(out=sign[:, :], in0=sign[:, :], in1=bit[:, :],
                                                       op=ALU.bitwise_and))
                    nc.vector.tensor_tensor(out=prefix[:, :], in0=prefix[:, :], in1=sign[:, :], op=ALU.bitwise_or)
                    chain.link(nc.vector.tensor_single_scalar(out=bit[:, :], in_=bit[:, :], scalar=1,
                                                              op=ALU.logical_shift_right))

                def a(c, s):
                    for f in range(FS):
                        for r in range(PER):
                            if r * FS // PER == f:
                                if r:
                                    answer(c * PER + r - 1)
                                ask(c * PER + r)
                        dve.wait_ge(u_ready, (c + 2) * FS + f + 1)
                        dve.wait_ge(silu_ready, c * FS + f + 1)
                        n = (s * FS + f) % 2
                        nc.vector.tensor_tensor(out=act_sb[:, s, f, :], in0=pu[n][:, :], in1=sg[:, n, :],
                                                op=ALU.mult).then_inc(gated, 1)
                    answer(c * PER + PER - 1)

                def b(c, s):
                    dve.wait_ge(down_ready, c + 1)
                    dve.wait_ge(h_loaded[s], (c - s) * 8 + 16)
                    for m in range(2):
                        last = nc.vector.tensor_tensor(out=h[:, s, 2 * m:2 * m + 2, :], in0=pd[m][:, :, :],
                                                       in1=h[:, s, 2 * m:2 * m + 2, :], op=ALU.add)
                    last.then_inc(sum_ready, 1)

                in_two_stages(nc.vector, NC, a, b)
                chain = Chain(dve, step, first + ROUNDS * LINKS)
                as_logit(chain, prefix[:, :])
                threshold = key[:, :].bitcast(F32)
                chain.link(nc.vector.tensor_scalar(out=gt[:, :], in0=z[:, :], scalar1=threshold, scalar2=None,
                                                   op0=ALU.is_gt, op1=ALU.add, accum_out=cnt[:, 0:1]))
                nc.vector.tensor_scalar(out=eq[:, :], in0=z[:, :], scalar1=threshold, scalar2=None, op0=ALU.is_equal,
                                        op1=ALU.add, accum_out=cnt[:, 1:2]).then_inc(counted, 1)
                dve.wait_ge(counted, ROUNDS + 1)
                chain.link(nc.vector.tensor_tensor_scan(out=rank[:, :], data0=eq[:, :], data1=eq[:, :], initial=0.0,
                                                        op0=ALU.add, op1=ALU.max))
                dve.wait_ge(totalled, ROUNDS + 1)
                chain.link(nc.vector.tensor_tensor(out=few[:, :], in0=few[:, :], in1=pc[:, 0:1], op=ALU.subtract))
                chain.link(nc.vector.tensor_tensor(out=few[:, :], in0=few[:, :], in1=pc[:, 1:2], op=ALU.subtract))
                chain.link(nc.vector.scalar_tensor_tensor(out=eq[:, :], in0=rank[:, :], scalar=few[:, :], in1=eq[:, :],
                                                          op0=ALU.is_le, op1=ALU.mult))
                chain.link(nc.vector.tensor_tensor(out=gt[:, :], in0=gt[:, :], in1=eq[:, :], op=ALU.add))
                chain.link(nc.vector.tensor_tensor_scan(out=rank[:, :], data0=gt[:, :], data1=gt[:, :], initial=0.0,
                                                        op0=ALU.add, op1=ALU.max))
                nc.vector.tensor_copy(cnt[:, 0:1], rank[:, L - 1:L]).then_inc(counted, 1)
                dve.wait_ge(totalled, ROUNDS + 2)
                chain.link(nc.vector.tensor_scalar(out=rank[:, :], in0=rank[:, :], scalar1=pc[:, 0:1], scalar2=None,
                                                   op0=ALU.add))
                nc.vector.tensor_copy(ct[:, :], rank[:, P - 1:L:P]).then_inc(c_ready, 1)


def experts(nc, NT, E, CAP, w_g, w_u, w_d, xs_d, c_d, ct_d, out):
    KC = CAP // P
    NW = min(CH, CAP)
    NH = CAP // NW
    KH = NW // P
    KP = KC // 2
    FS = w_d.shape[1] // P
    F = FS * P
    W = D + E
    with ExitStack() as ctx:
        sb = lambda name, shape, dt: ctx.enter_context(nc.sbuf_tensor(name, shape, dt))
        pb = lambda name, shape, dt: ctx.enter_context(nc.psum_tensor(name, shape, dt))
        sem = lambda name: ctx.enter_context(nc.semaphore(name))
        counts = sb("counts", [P, E + AHEAD, NT], F32)
        slot = sb("slot", [P, KC], F32)
        tile_le = sb("tile_le", [P, KC, NT], F32)
        tile = sb("tile", [P, 2, KC], F32)
        first_row = sb("first_row", [P, 1], F32)
        tile_row = sb("tile_row", [P, 2, KC], I32)
        run = sb("run", [P, 2, KC, P], F32)
        place = sb("place", [P, KC], F32)
        token = sb("token", [P, 2, KC], I32)
        target = sb("target", [P, 2, KC], I32)
        rows = sb("rows", [P, 2, KC, W], F32)
        scale = sb("scale", [P, 2, KC], F32)
        ident = sb("ident5", [P, P], F32)
        x1 = sb("x51", [P, 2, CAP], F32)
        x2 = sb("x52", [D2, 2, CAP], F32)
        wg1 = sb("wg1", [P, 2, F], F32)
        wg2 = sb("wg2", [D2, 2, F], F32)
        wu1 = sb("wu1", [P, 2, F], F32)
        wu2 = sb("wu2", [D2, 2, F], F32)
        wd = sb("wd", [P, 2, FS, D], F32)
        sg = sb("sg5", [P, 2, NW], F32)
        gu = sb("gu", [P, FS, CAP], F32)
        y = sb("y", [P, 2, KC, D], F32)
        pg = [pb(f"eg{m}", [P, CH], F32) for m in range(2)]
        pu = [pb(f"eu{m}", [P, CH], F32) for m in range(2)]
        pd = [pb(f"ed{m}", [P, 2, D], F32) for m in range(2)]
        t1 = pb("et1", [P, CH], F32)
        t2 = pb("et2", [D2, CH], F32)
        (made, counts_loaded, tile_ready, place_ready, target_ready, scaled, turned, x_ready, g_ready, silu_ready,
         u_ready, gated, down_ready, y_ready, step, passed) = (
            sem(n) for n in ("made5 counts_loaded tile_ready place_ready target_ready scaled turned5 x_ready5 g_ready5 "
                             "silu_ready5 u_ready5 gated5 down_ready5 y_ready step5 passed5").split())
        w_loaded, run_loaded, rows_loaded, added = ([sem(f"{n}{s}") for s in range(2)] for n in
                                                    ("w_loaded5", "run_loaded", "rows_loaded", "added"))
        with nc.Block() as block:
            @block.sync
            def _(sp):
                sp.dma_start(counts[:, :, :], ct_d.rearrange("(a e t) -> a e t", a=1, t=NT).broadcast_to(
                    [P, E + AHEAD, NT])).then_inc(counts_loaded, 16)

                def load(n, s):
                    for dst, src in ((wg1[:, s, :], w_g[bass.ds(n, 1), 0:P, :]), (wg2[:, s, :], w_g[bass.ds(n, 1), P:D, :]),
                                     (wu1[:, s, :], w_u[bass.ds(n, 1), 0:P, :]), (wu2[:, s, :], w_u[bass.ds(n, 1), P:D, :]),
                                     (wd[:, s, :, :], w_d[bass.ds(n, 1), :, :].rearrange("a (f p) d -> p (a f) d", p=P))):
                        sp.dma_start(dst, src if len(src.shape) == len(dst.shape) else
                                     src.rearrange("a p n -> (a p) n")).then_inc(w_loaded[s], 16)

                for s in range(2):
                    load(s, s)
                with nc.sync.Fori(1, E // 2) as i:
                    for s in range(2):
                        sp.wait_ge(down_ready, (i * 2 + s - 1) * KP)
                        hold(sp, passed)
                        load(i * 2 + s, s)

            @block.gpsimd
            def _(pool):
                def fetch_runs(n, s):
                    pool.wait_ge(tile_ready, n + 1)
                    hold(pool, passed)
                    for c in range(KC):
                        nc.gpsimd.indirect_dma_start(
                            out=run[:, s, c, :], out_offset=None, in_=c_d,
                            in_offset=bass.IndirectOffsetOnAxis(ap=tile_row[:, s, c:c + 1], axis=0),
                        ).then_inc(run_loaded[s], 16)

                def fetch_rows(n, s):
                    pool.wait_ge(place_ready, n + 1)
                    pool.wait_ge(turned, (n + 1) * NH)
                    pool.wait_ge(scaled, n + 1)
                    hold(pool, passed)
                    for c in range(KC):
                        nc.gpsimd.indirect_dma_start(
                            out=rows[:, s, c, :], out_offset=None, in_=xs_d,
                            in_offset=bass.IndirectOffsetOnAxis(ap=token[:, s, c:c + 1], axis=0),
                        ).then_inc(rows_loaded[s], 16)

                def add_results(n, s):
                    pool.wait_ge(y_ready, (n + 1) * KP + 2)
                    if not (isinstance(n, int) and n == 0):
                        pool.wait_ge(added[1 - s], (n - s) * (8 * KC) + 16 * KC * s)
                    hold(pool, passed)
                    for c in range(KC):
                        nc.gpsimd.indirect_dma_start(
                            out=out, out_offset=bass.IndirectOffsetOnAxis(ap=target[:, s, c:c + 1], axis=0),
                            in_=y[:, s, c, :], in_offset=None, compute_op=ALU.add).then_inc(added[s], 16)

                make_identity(nc, pool, ident, made)
                nc.gpsimd.iota(slot[:, :], pattern=[[P, KC]], base=0, channel_multiplier=1,
                               allow_small_or_imprecise_dtypes=True).then_inc(made, 1)
                fetch_runs(0, 0)
                fetch_runs(1, 1)
                fetch_rows(0, 0)

                def pair(i):
                    for s in range(2):
                        n = i * 2 + s
                        fetch_rows(n + 1, 1 - s)
                        fetch_runs(n + 2, s)
                        add_results(n, s)

                pair(0)
                with nc.gpsimd.Fori(1, E // 2) as i:
                    pair(i)
                for s in range(2):
                    pool.wait_ge(added[s], 16 * KC * (E // 2))

            @block.tensor
            def _(pe):
                pe.wait_ge(made, 2)
                pe.sem_inc(turned, 2 * NH)

                def turn(n, s, half):
                    if half == 0:
                        pe.wait_ge(rows_loaded[s], (n - s) * (8 * KC) + 16 * KC)
                    pe.wait_ge(x_ready, n * NH + half + 1)
                    for j in range(KH):
                        nc.tensor.transpose(t1[:, j * P:(j + 1) * P], rows[:, s, half * KH + j, 0:P], ident[:, :])
                    for j in range(KH):
                        last = nc.tensor.transpose(t2[:, j * P:(j + 1) * P], rows[:, s, half * KH + j, P:D],
                                                   ident[:, :])
                    last.then_inc(turned, 1)

                def up(n, s, half):
                    cols = slice(half * NW, (half + 1) * NW)
                    for f in range(FS):
                        m = f % 2
                        pe.wait_ge(gated, (n * NH + half) * FS + f + 1)
                        fs = slice(f * P, (f + 1) * P)
                        for w1, w2, o, done in ((wg1, wg2, pg, g_ready), (wu1, wu2, pu, u_ready)):
                            nc.tensor.matmul(o[m][:, 0:NW], w1[:, s, fs], x1[:, s, cols], start=True, stop=False)
                            nc.tensor.matmul(o[m][:, 0:NW], w2[:, s, fs], x2[:, s, cols], start=False,
                                             stop=True).then_inc(done, 1)

                def down(n, s, pair):
                    if pair * 2 % KH == 0:
                        pe.wait_ge(gated, (n * NH + pair * 2 // KH + 1) * FS + 2)
                    pe.wait_ge(y_ready, n * KP + pair + 1)
                    for j in range(2):
                        t = pair * 2 + j
                        for f in range(FS):
                            last = nc.tensor.matmul(pd[(s * KP + pair) % 2][:, j, :], gu[:, f, t * P:(t + 1) * P],
                                                    wd[:, s, f, :], start=(f == 0), stop=(f == FS - 1))
                    last.then_inc(down_ready, 1)

                for half in range(NH):
                    turn(0, 0, half)
                with nc.tensor.Fori(0, E // 2) as i:
                    for s in range(2):
                        n = i * 2 + s
                        pe.wait_ge(w_loaded[s], (i + 1) * 80)
                        pe.wait_ge(x_ready, (n + 1) * NH + 1)
                        for half in range(NH):
                            up(n, s, half)
                        for pair in range(KP):
                            if pair >= KP - NH:
                                turn(n + 1, 1 - s, pair - (KP - NH))
                            down(n, s, pair)

            @block.scalar
            def _(act):
                act.sem_inc(x_ready, 1)

                def move(n, s):
                    for half in range(NH):
                        cols = slice(half * NW, (half + 1) * NW)
                        act.wait_ge(turned, (n + 2) * NH + half + 1)
                        nc.scalar.activation(x1[:, s, cols], t1[:, 0:NW], ACT.Copy)
                        nc.scalar.activation(x2[:, s, cols], t2[:, 0:NW], ACT.Copy).then_inc(x_ready, 1)

                move(0, 0)
                with nc.scalar.Fori(0, E // 2) as i:
                    for s in range(2):
                        n = i * 2 + s
                        for half in range(NH):
                            for f in range(FS):
                                u = (n * NH + half) * FS + f
                                act.wait_ge(g_ready, u + 1)
                                act.wait_ge(gated, u + 1)
                                nc.scalar.activation(sg[:, f % 2, :], pg[f % 2][:, 0:NW], ACT.Silu).then_inc(
                                    silu_ready, 1)
                        move(n + 1, 1 - s)

            @block.vector
            def _(dve):
                dve.sem_inc(scaled, 2)
                dve.sem_inc(gated, 2)
                dve.sem_inc(y_ready, 2)
                chain = Chain(dve, step)
                chain.link(nc.vector.memset(first_row[:, :], 0.0))
                dve.wait_ge(made, 3)
                dve.wait_ge(counts_loaded, 16)

                def compare_tiles(n, chain):
                    chain.link(nc.vector.tensor_tensor(
                        out=tile_le[:, :, :], in0=counts[:, bass.ds(n, 1), :].broadcast_to([P, KC, NT]),
                        in1=slot[:, :].unsqueeze(2).broadcast_to([P, KC, NT]), op=ALU.is_le))

                def find_tile(n, s, chain):
                    chain.link(nc.vector.tensor_reduce(out=tile[:, s, :], in_=tile_le[:, :, :], op=ALU.add, axis=AX.X))
                    chain.link(nc.vector.tensor_scalar(out=tile_row[:, s, :], in0=tile[:, s, :],
                                                       scalar1=first_row[:, :], scalar2=None, op0=ALU.add))
                    dve.sem_inc(tile_ready, 1)
                    chain.link(nc.vector.tensor_scalar(out=first_row[:, :], in0=first_row[:, :], scalar1=float(NT),
                                                       scalar2=None, op0=ALU.add))

                def compare_places(n, s, chain):
                    dve.wait_ge(run_loaded[s], (n - s) * (8 * KC) + 16 * KC)
                    chain.link(nc.vector.tensor_tensor(out=run[:, s, :, :], in0=run[:, s, :, :],
                                                       in1=slot[:, :].unsqueeze(2).broadcast_to([P, KC, P]),
                                                       op=ALU.is_le))

                def find_token(n, s, chain):
                    chain.link(nc.vector.tensor_reduce(out=place[:, :], in_=run[:, s, :, :], op=ALU.add, axis=AX.X))
                    chain.link(nc.vector.scalar_tensor_tensor(out=token[:, s, :], in0=tile[:, s, :], scalar=float(P),
                                                              in1=place[:, :], op0=ALU.mult, op1=ALU.add))
                    dve.sem_inc(place_ready, 1)

                for n in range(AHEAD):
                    compare_tiles(n, chain)
                    find_tile(n, n % 2, chain)
                    if n:
                        compare_places(n - 1, (n - 1) % 2, chain)
                        find_token(n - 1, (n - 1) % 2, chain)
                first, LINKS = chain.n, 9

                def gate(n, half, f):
                    u = (n * NH + half) * FS + f
                    dve.wait_ge(u_ready, u + 1)
                    dve.wait_ge(silu_ready, u + 1)
                    nc.vector.tensor_tensor(out=gu[:, f, half * NW:(half + 1) * NW], in0=pu[f % 2][:, 0:NW],
                                            in1=sg[:, f % 2, :], op=ALU.mult).then_inc(gated, 1)

                def pair(i):
                    for s in range(2):
                        n = i * 2 + s
                        chain = Chain(dve, step, first + n * LINKS)
                        dve.wait_ge(rows_loaded[s], (n - s) * (8 * KC) + 16 * KC)
                        chain.link(nc.vector.tensor_copy(scale[:, s, :].unsqueeze(2),
                                                         rows[:, s, :, bass.ds(n + D, 1)]))
                        dve.sem_inc(scaled, 1)
                        if not isinstance(i, int):
                            dve.wait_ge(added[s], (n - s) * (8 * KC))
                        chain.link(nc.vector.tensor_copy(target[:, s, :], token[:, s, :]))
                        for half in range(NH):
                            for f in range(FS):
                                gate(n, half, f)
                                if half == NH - 1:
                                    if f == 0:
                                        compare_places(n + 2, s, chain)
                                    elif f == 1:
                                        find_token(n + 2, s, chain)
                                    elif f == 2:
                                        compare_tiles(n + 3, chain)
                                    elif f == 3:
                                        find_tile(n + 3, 1 - s, chain)
                        assert chain.n == LINKS, chain.n
                        for m in range(KP):
                            dve.wait_ge(down_ready, n * KP + m + 1)
                            nc.vector.tensor_tensor(
                                out=y[:, s, 2 * m:2 * m + 2, :], in0=pd[(s * KP + m) % 2][:, :, :],
                                in1=scale[:, s, 2 * m:2 * m + 2].unsqueeze(2).broadcast_to([P, 2, D]),
                                op=ALU.mult).then_inc(y_ready, 1)

                pair(0)
                with nc.vector.Fori(1, E // 2) as i:
                    pair(i)


def tower(nc, x, token_emb, instr_emb, arg_emb, norm_w, norm_b, w_qkv, b_qkv, w_out, b_out, gate, w_g, w_u, w_d, ws_g,
          ws_u, ws_d, out):
    B, S = x.shape
    E = w_g.shape[0]
    n_tok = B * S
    NT = n_tok // P
    CAP = -(-n_tok * 2 // E)
    h_d = nc.dram_tensor("h_d", [n_tok, D], F32).ap()
    qk_d = nc.dram_tensor("qk_d", [3, 2 * D, n_tok], BF16).ap()
    xs_d = nc.dram_tensor("xs_d", [n_tok, D + E], F32).ap()
    xt_d = nc.dram_tensor("xt_d", [D, n_tok], F32).ap()
    c_d = nc.dram_tensor("c_d", [(E + AHEAD) * NT, P], F32).ap()
    ct_d = nc.dram_tensor("ct_d", [(E + AHEAD) * NT], F32).ap()
    with nc.sbuf_tensor("z_all", [P, NT, E], F32) as z_all:
        with nc.sbuf_tensor("attn", [P, NT, D], F32) as attn:
            with nc.sbuf_tensor("v_all", [P, NT, D], F32) as v_all:
                with nc.sbuf_tensor("idx", [P, 3, NT], I32) as idx:
                    positions(nc, B, S, x, idx)
                    embed_and_project(nc, NT, (token_emb, instr_emb, arg_emb), norm_w, norm_b, w_qkv, b_qkv, idx, h_d,
                                      qk_d, v_all)
                attention(nc, B, S, qk_d, v_all, attn)
            project_and_gate(nc, NT, E, attn, w_out, b_out, gate, h_d, xs_d, xt_d, z_all)
        shared_and_choose(nc, NT, E, CAP, ws_g, ws_u, ws_d, h_d, xs_d, xt_d, z_all, out, c_d.rearrange("a b -> (a b)"),
                          ct_d)
    experts(nc, NT, E, CAP, w_g, w_u, w_d, xs_d, c_d, ct_d, out)


def kernel(**inputs):
    import numpy as np
    import concourse.bacc as bacc
    from concourse.bass_utils import run_bass_kernel_spmd

    nc = bacc.Bacc("TRN2", target_bir_lowering=False, num_devices=1)
    given = {n: np.asarray(a) for n, a in inputs.items()}
    arrays = {
        "x": given["x"],
        "token_emb": given["L0_tok_token_emb"],
        "instr_emb": given["L0_tok_instr_emb"],
        "arg_emb": given["L0_tok_arg_emb"],
        "norm_w": given["L0_tok_norm_w"],
        "norm_b": given["L0_tok_norm_b"],
        "w_qkv": given["L0_attn_w_qkv"].T,
        "b_qkv": given["L0_attn_b_qkv"],
        "w_out": given["L0_attn_w_out"].T,
        "b_out": given["L0_attn_b_out"],
        "gate": given["L0_ffn_gate_weight"].T,
        "w_g": given["L0_ffn_Wg"].transpose(0, 2, 1),
        "w_u": given["L0_ffn_Wu"].transpose(0, 2, 1),
        "w_d": given["L0_ffn_Wd"].transpose(0, 2, 1),
        "ws_g": given["L0_ffn_Ws_g"].T,
        "ws_u": given["L0_ffn_Ws_u"].T,
        "ws_d": given["L0_ffn_Ws_d"].T,
    }
    arrays = {n: np.ascontiguousarray(a) for n, a in arrays.items()}
    args = [nc.dram_tensor(n, a.shape, mybir.dt.from_np(a.dtype), kind="ExternalInput").ap() for n, a in arrays.items()]
    B, S = arrays["x"].shape
    out = nc.dram_tensor("out", (B * S, D), F32, kind="ExternalOutput").ap()
    tower(nc, *args, out)
    result = run_bass_kernel_spmd(nc, [arrays], core_ids=[0])
    return result.results[0]["out"].reshape(B, S, D)
```
